# Optimizing a Trainium2 kernel written in Bass

```python
import numpy as np
import jax
import jax.numpy as jnp

def _softmax(x, axis=-1):
    return jax.nn.softmax(x, axis=axis)

def _gelu(x):
    return jax.nn.gelu(x, approximate=True)

def _silu(x):
    return jax.nn.silu(x)

def _sigmoid(x):
    return jax.nn.sigmoid(x)

def _layernorm(x, axis=-1, eps=1e-05):
    m = jnp.mean(x, axis=axis, keepdims=True)
    v = jnp.var(x, axis=axis, keepdims=True)
    return (x - m) / jnp.sqrt(v + eps)

def _scatter_add(tgt, idx, src, axis=0):
    return tgt.at[idx].add(src)

def _segment_sum(src, seg, n):
    return jax.ops.segment_sum(src, seg, n)
kernel_name = 'mk_xattn_ffn_d1_seqx_r2_b63e39'

def setup_inputs(seed: int=0):
    np.random.seed(seed)
    _w = jnp.asarray

    def _rec_inputs():
        import jax
        import jax.numpy as jnp
        _rk = jax.random.key(seed)
        x = -0.000125 + 0.9999 * jax.random.normal(jax.random.fold_in(_rk, 1), (8, 1024, 1024), jnp.float32)
        _lenS = 1024 - jax.random.randint(jax.random.fold_in(_rk, 7), (8,), 0, max(1, 1024 // 4) + 1, jnp.int32)
        _lenS2 = 64 - jax.random.randint(jax.random.fold_in(_rk, 8), (8,), 0, max(1, 64 // 4) + 1, jnp.int32)
        _ctx_2048P = jax.random.normal(jax.random.fold_in(_rk, 11), (8, 16, 1024), jnp.float32)
        _ctx_2048c = jax.random.dirichlet(jax.random.fold_in(_rk, 511), 0.3 * jnp.ones((16,), jnp.float32), (8, 64))
        _ctx_2048t = jnp.einsum('bsk,bkd->bsd', _ctx_2048c, _ctx_2048P)
        _ctx_2048t = _ctx_2048t * jax.lax.rsqrt(jnp.mean(jnp.square(_ctx_2048t)) + 1e-12) * 0.953939
        ctx_2048 = -0.000514642 + 1.00011 * (_ctx_2048t + 0.3 * jax.random.normal(jax.random.fold_in(_rk, 611), (8, 64, 1024), jnp.float32))
        _validS = jnp.arange(1024)[None, :] < _lenS[:, None]
        _validS2 = jnp.arange(64)[None, :] < _lenS2[:, None]
        _causal = jnp.tril(jnp.ones((1024, 1024), dtype=bool))
        mask_BxS2_bk0 = jnp.logical_not(jnp.broadcast_to(_validS2[:, :], (8, 64)))
        return (x, ctx_2048, mask_BxS2_bk0)
    x, ctx_2048, mask_BxS2_bk0 = _rec_inputs()

    def _L0_xattn_setup():
        import jax, jax.numpy as jnp
        import numpy as np
        key = jax.random.key(seed)
        k1, k2, k3 = jax.random.split(key, 3)
        B, S, D, M = (8, 1024, 1024, 128)
        hidden_states = jax.random.normal(k1, (B, S, D), dtype=jnp.float32)
        memory_tokens = jax.random.normal(k2, (B, M, D), dtype=jnp.float32)
        memory_mask = jax.random.randint(k3, (B, M), 0, 2).astype(jnp.bool_)
        return {'hidden_states': hidden_states, 'memory_tokens': memory_tokens, 'memory_mask': memory_mask}
    _L0_xattn_all = _L0_xattn_setup()
    _L0_xattn_in = {k: v for k, v in _L0_xattn_all.items() if k in ()}
    del _L0_xattn_all

    def _L0_ffn_setup():
        import math
        import jax, jax.numpy as jnp
        import numpy as np
        DIM = 1024
        RANK = 8
        B, T = (4, 2048)

        def _orthogonal(key, n):
            a = jax.random.normal(key, (n, n), dtype=jnp.float32)
            q, r = jnp.linalg.qr(a)
            q = q * jnp.sign(jnp.diagonal(r))[None, :]
            return q
        key = jax.random.key(seed)
        kx, kf = jax.random.split(key)
        x = jax.random.normal(kx, (B, T, DIM), dtype=jnp.float32)
        fkeys = jax.random.split(kf, RANK)
        factors = jnp.stack([_orthogonal(fkeys[r], DIM) * (r + 1) ** (-0.5) for r in range(RANK)])
        bias = jnp.zeros((DIM,), dtype=jnp.float32)
        return {'x': x, 'factors': factors, 'bias': bias}
    _L0_ffn_all = _L0_ffn_setup()
    _L0_ffn_in = {k: v for k, v in _L0_ffn_all.items() if k in ('factors', 'bias')}
    del _L0_ffn_all
    return {'x': x, 'ctx_2048': ctx_2048, 'mask_BxS2_bk0': mask_BxS2_bk0, 'L0_ffn_factors': _L0_ffn_in['factors'], 'L0_ffn_bias': _L0_ffn_in['bias']}

def reference(x, ctx_2048, mask_BxS2_bk0, L0_ffn_factors, L0_ffn_bias):
    import jax
    import jax.numpy as jnp

    def _L0_xattn_ref(hidden_states, memory_tokens, memory_mask):
        import jax, jax.numpy as jnp
        import numpy as np
        B, S, D = hidden_states.shape
        scale = 1.0 / jnp.sqrt(jnp.asarray(D, hidden_states.dtype))
        scores = jnp.einsum('bsd,bmd->bsm', hidden_states, memory_tokens) * scale
        neg_inf = jnp.asarray(-1e+30, scores.dtype)
        scores = jnp.where(memory_mask[:, None, :], scores, neg_inf)
        attn = jax.nn.softmax(scores, axis=-1)
        readout = jnp.einsum('bsm,bmd->bsd', attn, memory_tokens)
        valid_b = jnp.any(memory_mask, axis=-1)
        out = jnp.where(valid_b[:, None, None], readout, jnp.zeros_like(readout))
        return out

    def _L0_ffn_ref(x, factors, bias):
        import math
        import jax, jax.numpy as jnp
        import numpy as np
        DIM = 1024
        RANK = 8
        B, T = (4, 2048)

        def _orthogonal(key, n):
            a = jax.random.normal(key, (n, n), dtype=jnp.float32)
            q, r = jnp.linalg.qr(a)
            q = q * jnp.sign(jnp.diagonal(r))[None, :]
            return q
        rank = factors.shape[0]
        mixed = jnp.einsum('btd,rde->bte', x, factors)
        mixed = mixed / math.sqrt(rank) + bias
        return mixed
    x = x + _L0_xattn_ref(_layernorm(x, axis=-1), ctx_2048, mask_BxS2_bk0)
    x = x + _L0_ffn_ref(_layernorm(x, axis=-1), L0_ffn_factors, L0_ffn_bias)
    return x

_drawn_inputs = setup_inputs


def setup_inputs(seed=0):
    import zlib

    import numpy as np

    out = dict(_drawn_inputs(seed))
    spreads = {'L0_ffn_bias': (0.0, 0.1)}
    factors = {}
    for name, (base, spread) in spreads.items():
        noise = np.random.default_rng([zlib.crc32(name.encode()), seed]).standard_normal(out[name].shape)
        drawn = base * np.exp(spread * noise) if base else spread * noise
        out[name] = jnp.asarray(drawn.astype(out[name].dtype))
    for name, factor in factors.items():
        out[name] = (out[name] * factor).astype(out[name].dtype)
    return out
```

```python
from contextlib import ExitStack

import concourse.bass as bass
from concourse import mybir

ALU = mybir.AluOpType
ACT = mybir.ActivationFunctionType
F32 = mybir.dt.float32
F32R = mybir.dt.float32r
F16 = mybir.dt.float16
U8 = mybir.dt.uint8
I32 = mybir.dt.int32
AX_X = mybir.AxisListType.X
RMAX = bass.bass_isa.ReduceOp.max

P = 128
D = 1024
M = 64
NB = 8
NT = 64
TB = NT // NB
C = D // P
NR = 8
QW = 256
NQ = D // QW
NX = 9
NXT = 8
NPRO = 7
NS = 3
NM = 3
NLD = 8
EPS = 1e-5
XS = 2.0 ** 10
WS_ = 2.0 ** 14
TINY = 2.0 ** -80


def schedule():
    items = []

    def step(k, mid=None):
        if k < NT:
            items.append(("ST", k))
        if 0 <= k - 2 < NT:
            items.append(("X1N", k - 2))
        if k < NT:
            if k % TB == 0:
                items.append(("CTX", k // TB))
            items.append(("XN", k))
        if mid:
            items.append(mid[0])
        if k < NT:
            items.append(("T1", k))
        if 0 <= k - 1 < NT:
            items.append(("T2", k - 1))
        if mid and mid[1]:
            items.append(mid[1])
        if 0 <= k - 2 < NT:
            items.append(("T3", k - 2))
        if k < NT:
            items.append(("S", k))
        if 0 <= k - 1 < NT:
            items.append(("R", k - 1))

    for k in range(4):
        items.append(("WP", 2 * k))
        items.append(("WP", 2 * k + 1))
        step(k)
    items.append(("CVT", 0))
    for q in range(NQ - 1):
        for j in range(C):
            items.append(("WD", (q + 1) * C + j))
            if j < NPRO:
                items.append(("U", j, q * QW, QW))
            if q == 0 and 4 + j < NX:
                step(4 + j)
        items.append(("CVT", q + 1))
    k = NX
    for i in range(NPRO):
        items.append(("U", i, (NQ - 1) * QW, QW))
        if i in (3, 5):
            step(k)
            k += 1
    for i in range(NPRO, NT):
        step(k, (("U", i, 0, 512), ("U", i, 512, 512)))
        k += 1
    return items


def xattn_ffn_kernel(nc, x, ctx_in, mask, fac, bias, out):
    items = schedule()
    tp_use, mi_use, mn_use, units = {}, {}, {}, {}
    n_tp = n_mi = n_mn = 0
    for it in items:
        if it[0] in ("T1", "T3"):
            tp_use[it] = n_tp
            n_tp += 2
        elif it[0] == "CTX":
            tp_use[it] = n_tp
            n_tp += 1
        if it[0] in ("S", "T2", "CTX"):
            mi_use[it] = n_mi
            n_mi += 1
        if it[0] in ("WP", "U"):
            mn_use[it] = n_mn
            if it[0] == "U":
                units[it[1]] = n_mn
            n_mn += 1
    for it in items:
        assert items.count(it) == 1
    wd_done = {}
    for it in items:
        if it[0] == "WD":
            wd_done[it[1]] = len(wd_done) + 1

    with ExitStack() as ctx:
        def sb(name, shape, dt):
            return ctx.enter_context(nc.sbuf_tensor(name, shape, dt))

        def ps(name, shape, dt):
            return ctx.enter_context(nc.psum_tensor(name, shape, dt))

        def sem(name):
            return ctx.enter_context(nc.semaphore(name))

        WH = sb("WH", [P, C, D], F16)
        WL = sb("WL", [P, C, D], F16)
        WG = sb("WG", [P, NS, NR, QW], F32)
        WF = sb("WF", [P, 2, C, QW], F32)
        X = sb("X", [P, NX, D], F32)
        XN = sb("XN", [P, D], F32)
        X1N = sb("X1N", [P, D], F32)
        XH = sb("XH", [P, C, P], F16)
        XL = sb("XL", [P, C, P], F16)
        YH = sb("YH", [P, NXT, C, P], F16)
        YL = sb("YL", [P, NXT, C, P], F16)
        CX = sb("CX", [P, D], F32)
        CS = sb("CS", [M, D], F32)
        CH = sb("CH", [P, 2, D], F32R)
        CL = sb("CL", [M, 2, D], F32R)
        CTH = sb("CTH", [P, 2, C, M], F16)
        CTL = sb("CTL", [P, 2, C, M], F16)
        BI = sb("BI", [P, D], F32)
        MU = sb("MU", [P, NB, M], U8)
        MF = sb("MF", [P, NB, M], F32)
        NG = sb("NG", [P, NB, M], F32)
        VA = sb("VA", [P, NB], F32)
        SMU = sb("SMU", [P, 2, M], F32)
        DG = sb("DG", [M, M], F32)
        ID = sb("ID", [P, P], F32)
        ONE = sb("ONE", [P, P], F32)
        PW = sb("PW", [P, 1], F32)
        TA = sb("TA", [P, M], F32)
        TC = sb("TC", [P, M], F32)
        TD = sb("TD", [P, M], F32)
        MX = sb("MX", [P, 1], F32)
        PP = sb("PP", [P, 2 * M], F32)
        PA = sb("PA", [P, P], F32R)
        SM = sb("SM", [P, 4], F32)
        RC = sb("RC", [P, 1], F32)
        B1 = sb("B1", [P, 2, 6], F32)
        B2 = sb("B2", [P, 2, 6], F32)
        V1 = sb("V1", [P, 4, 4], F32)
        V2 = sb("V2", [P, 4, 4], F32)
        G1 = sb("G1", [P, 4, 2], F32)
        G2 = sb("G2", [P, 4, 2], F32)
        AM = sb("AM", [P, NQ, C], F32)
        A1 = sb("A1", [P, NQ], F32)
        A2 = sb("A2", [P, NQ], F32)
        A3 = sb("A3", [P, NQ], F32)
        SW = sb("SW", [P, NQ], F32)
        AL = sb("AL", [P, NQ], F32)
        K1 = sb("K1", [M, 8], F32)

        MN = ps("MN", [P, NM, 512], F32)
        TP = ps("TP", [P, 2, 512], F32)
        RP = ps("RP", [P, 2, 512], F32)
        MI = ps("MI", [P, 512], F32)

        s_ld = [sem(f"s_ld{i}") for i in range(NX)]
        s_st = [sem(f"s_st{i}") for i in range(NX)]
        s_wg = [sem(f"s_wg{i}") for i in range(NS)]
        s_cx = sem("s_cx")
        s_bm = sem("s_bm")
        s_mk = sem("s_mk")
        s_id0 = sem("s_id0")
        s_id = sem("s_id")
        s_one = sem("s_one")
        s_v1 = sem("s_v1")
        s_v2 = sem("s_v2")
        s_p1 = sem("s_p1")
        s_p2 = sem("s_p2")
        s_xn = sem("s_xn")
        s_x1 = sem("s_x1")
        s_bi = sem("s_bi")
        s_tw = sem("s_tw")
        s_th = sem("s_th")
        s_tl = sem("s_tl")
        s_mw = sem("s_mw")
        s_mi = sem("s_mi")
        s_pe = sem("s_pe")
        s_mn = sem("s_mn")
        s_t4 = sem("s_t4")
        s_e = sem("s_e")
        s_pa = sem("s_pa")
        s_rw = sem("s_rw")
        s_rr = sem("s_rr")
        s_wd = sem("s_wd")
        s_ws = sem("s_ws")
        s_am = sem("s_am")
        s_ar = sem("s_ar")
        s_sw = sem("s_sw")
        s_wh = sem("s_wh")
        s_wl = sem("s_wl")
        s_c1 = sem("s_c1")
        s_cs = sem("s_cs")
        s_ch = sem("s_ch")
        s_cl = sem("s_cl")
        s_dg = sem("s_dg")
        s_vc = sem("s_vc")
        s_pc = sem("s_pc")

        xt = x.rearrange("b s d -> (b s) d").rearrange("(n p) d -> n p d", p=P)
        ot = out.rearrange("b s d -> (b s) d").rearrange("(n p) d -> n p d", p=P)
        ft = fac.rearrange("r (c p) (q e) -> q c p r e", p=P, e=QW)

        block = ctx.enter_context(nc.Block())

        @block.sync
        def _(sp):
            stored = [0]

            def load_x(j):
                if j >= NX:
                    sp.wait_ge(s_st[j % NX], 16 * (j // NX))
                sp.dma_start(X[:, j % NX, :], xt[j]).then_inc(s_ld[j % NX], 16)

            def load_ctx(b):
                if b:
                    sp.wait_ge(s_cl, b)
                    sp.wait_ge(s_ch, b)
                    sp.wait_ge(s_cs, b)
                sp.dma_start(CX[0:M, :], ctx_in[b]).then_inc(s_cx, 16)
                sp.dma_start(CX[M:P, :], ctx_in[b]).then_inc(s_cx, 16)

            def load_w(n):
                if n >= NS:
                    o = n - NS
                    if o in wd_done:
                        sp.wait_ge(s_wd, wd_done[o])
                    else:
                        sp.wait_ge(s_pe, mn_use[("WP", o)] + 1)
                sp.dma_start(WG[:, n % NS], ft[n // C, n % C]).then_inc(s_wg[n % NS], 16)

            def store(j):
                sp.wait_ge(s_mn, units[j] + 1)
                sp.dma_start(ot[j], X[:, j % NX, :]).then_inc(s_st[j % NX], 16)

            load_x(0)
            load_ctx(0)
            sp.dma_start(MU[:], mask.rearrange("b m -> (b m)").partition_broadcast(P)).then_inc(s_mk, 16)
            load_w(0)
            load_w(1)
            sp.dma_start(BI[:], bias.partition_broadcast(P)).then_inc(s_bm, 16)
            nx = 1
            for n in range(2, NQ * C):
                load_w(n)
                if (n in (2, 4, 6) or n > 7) and nx < NX:
                    load_x(nx)
                    nx += 1
                if n == 13:
                    load_ctx(1)
            for j in range(NT):
                store(j)
                if j + NX < NT:
                    load_x(j + NX)
                if (j + 7) % TB == 0 and 2 <= (j + 7) // TB < NB:
                    load_ctx((j + 7) // TB)
            for i in range(NX):
                sp.wait_ge(s_st[i], 16 * len(range(i, NT, NX)))

        @block.gpsimd
        def _(pool):
            nc.gpsimd.memset(ID[:], 0.0).then_inc(s_id0, 1)
            pool.wait_ge(s_id0, 1)
            nc.gpsimd.affine_select(out=ID[:], in_=ID[:], compare_op=ALU.not_equal, fill=1.0, base=0,
                                    pattern=[[-1, P]], channel_multiplier=1).then_inc(s_id, 1)
            nc.gpsimd.memset(ONE[:], 1.0).then_inc(s_one, 1)
            nc.gpsimd.memset(PW[:], -0.5).then_inc(s_pc, 1)
            chain = [1]
            pool.wait_ge(s_pc, 1)

            def scales(V, G, j, ready, done):
                pool.wait_ge(ready, j + 1)
                s = j % 4
                nc.gpsimd.tensor_tensor(G[:, s, 0:1], V[:, s, 3:4], PW[:], ALU.pow).then_inc(s_pc, 1)
                chain[0] += 1
                pool.wait_ge(s_pc, chain[0])
                nc.gpsimd.tensor_tensor(G[:, s, 1:2], V[:, s, 2:3], G[:, s, 0:1], ALU.mult).then_inc(done, 1)

            for it in items:
                if it[0] == "ST":
                    scales(V1, G1, it[1], s_v1, s_p1)
                elif it[0] == "R":
                    scales(V2, G2, it[1], s_v2, s_p2)
                elif it[0] == "X1N":
                    j = it[1]
                    if j == 0:
                        pool.wait_ge(s_bm, 16)
                    pool.wait_ge(s_x1, j + 1)
                    xs = X[:, j % NX, :]
                    nc.gpsimd.tensor_tensor(xs, xs, BI[:], ALU.add).then_inc(s_bi, 1)
                elif it[0] == "CVT":
                    q = it[1]
                    pool.wait_ge(s_am, q + 1)
                    nc.gpsimd.partition_all_reduce(A2[:, q:q + 1], A1[:, q:q + 1], P, RMAX).then_inc(s_ar, 1)

        @block.scalar
        def _(act):
            def high(n, dst, src):
                act.wait_ge(s_tw, n + 1)
                nc.scalar.activation(dst, src, ACT.Copy).then_inc(s_th, 1)

            for it in items:
                kind = it[0]
                j = it[1]
                if kind == "XN":
                    act.wait_ge(s_p1, j + 1)
                    act.wait_ge(s_ld[j % NX], 16 * (j // NX + 1))
                    if j:
                        act.wait_ge(s_tw, tp_use[("T1", j - 1)] + 2)
                    nc.scalar.activation(XN[:], X[:, j % NX, :], ACT.Identity, bias=G1[:, j % 4, 1:2],
                                         scale=G1[:, j % 4, 0:1]).then_inc(s_xn, 1)
                elif kind == "X1N":
                    act.wait_ge(s_p2, j + 1)
                    if j:
                        act.wait_ge(s_tw, tp_use[("T3", j - 1)] + 2)
                    nc.scalar.activation(X1N[:], X[:, j % NX, :], ACT.Identity, bias=G2[:, j % 4, 1:2],
                                         scale=G2[:, j % 4, 0:1]).then_inc(s_x1, 1)
                elif kind == "T1":
                    n = tp_use[it]
                    if j:
                        act.wait_ge(s_mw, mi_use[("S", j - 1)] + 1)
                    for h in range(2):
                        high(n + h, XH[:, 4 * h:4 * h + 4, :], TP[:, (n + h) % 2, :])
                elif kind == "T3":
                    n = tp_use[it]
                    if j >= NXT:
                        act.wait_ge(s_pe, units[j - NXT] + 1)
                    for h in range(2):
                        high(n + h, YH[:, j % NXT, 4 * h:4 * h + 4, :], TP[:, (n + h) % 2, :])
                elif kind == "S":
                    act.wait_ge(s_t4, j + 1)
                    if j:
                        act.wait_ge(s_mw, mi_use[("T2", j - 1)] + 1)
                    nc.scalar.activation(PP[:, 0:M], TD[:], ACT.Exp,
                                         accum_out=SM[:, j % 4:j % 4 + 1]).then_inc(s_e, 1)
                    nc.scalar.activation(PP[:, M:2 * M], TD[:], ACT.Exp).then_inc(s_e, 1)
                elif kind == "T2":
                    act.wait_ge(s_mw, mi_use[it] + 1)
                    if j:
                        act.wait_ge(s_rw, 2 * j)
                    nc.scalar.activation(PA[:], MI[:, 0:P], ACT.Copy).then_inc(s_pa, 1)
                elif kind == "WP":
                    m = mn_use[it]
                    q, c = divmod(j, C)
                    act.wait_ge(s_pe, m + 1)
                    if q >= 2:
                        act.wait_ge(s_wl, q - 1)
                    nc.scalar.activation(WF[:, q % 2, c, :], MN[:, m % NM, 0:QW], ACT.Copy).then_inc(s_ws, 1)
                elif kind == "CVT":
                    q = j
                    act.wait_ge(s_sw, q + 1)
                    nc.scalar.activation(WH[:, :, q * QW:(q + 1) * QW], WF[:, q % 2], ACT.Copy,
                                         scale=SW[:, q:q + 1]).then_inc(s_wh, 1)
                elif kind == "CTX":
                    b = j
                    act.wait_ge(s_c1, b + 1)
                    if b:
                        act.wait_ge(s_tw, tp_use[("CTX", b - 1)] + 1)
                    nc.scalar.activation(CS[:], CX[0:M, :], ACT.Copy, scale=K1[:, 4:5]).then_inc(s_cs, 1)
                    act.wait_ge(s_cx, 32 * (b + 1))
                    if b >= 2:
                        act.wait_ge(s_rw, 2 * TB * (b - 1))
                    nc.scalar.activation(CH[:, b % 2, :], CX[:], ACT.Copy, scale=VA[:, b:b + 1]).then_inc(s_ch, 1)
                    n = tp_use[it]
                    high(n, CTH[:, b % 2], TP[:, n % 2, :])

        @block.vector
        def _(dve):
            chain = [0]

            def link(ins):
                chain[0] += 1
                ins.then_inc(s_vc, 1)
                dve.wait_ge(s_vc, chain[0])

            def low(n, dst, src, hi):
                dve.wait_ge(s_th, n + 1)
                nc.vector.tensor_tensor(dst, src, hi, ALU.subtract).then_inc(s_tl, 1)

            def stats(B, V, j, src, done):
                for h in range(2):
                    last = nc.vector.bn_stats(B[:, h, :], src[:, 512 * h:512 * h + 512])
                link(last)
                s = j % 4
                link(nc.vector.bn_aggr(V[:, s, 0:2], B[:]))
                nc.vector.tensor_scalar(V[:, s, 2:3], V[:, s, 0:1], -1.0, None, ALU.mult)
                nc.vector.tensor_scalar(V[:, s, 3:4], V[:, s, 1:2], EPS, XS ** -2, ALU.add,
                                        ALU.mult).then_inc(done, 1)

            dve.wait_ge(s_mk, 16)
            link(nc.vector.tensor_copy(MF[:], MU[:]))
            nc.vector.tensor_scalar(NG[:], MF[:], -1.0, 1e30, ALU.add, ALU.mult)
            link(nc.vector.tensor_reduce(VA[:], MF[:], AX_X, ALU.max))
            dve.wait_ge(s_id, 1)

            for it in items:
                kind = it[0]
                j = it[1]
                if kind == "ST":
                    dve.wait_ge(s_ld[j % NX], 16 * (j // NX + 1))
                    stats(B1, V1, j, X[:, j % NX, :], s_v1)
                elif kind == "T1":
                    n = tp_use[it]
                    for h in range(2):
                        c = slice(4 * h, 4 * h + 4)
                        low(n + h, XL[:, c, :], TP[:, (n + h) % 2, :], XH[:, c, :])
                elif kind == "T3":
                    n = tp_use[it]
                    for h in range(2):
                        c = slice(4 * h, 4 * h + 4)
                        low(n + h, YL[:, j % NXT, c, :], TP[:, (n + h) % 2, :], YH[:, j % NXT, c, :])
                elif kind == "S":
                    b = j // TB
                    dve.wait_ge(s_mw, mi_use[it] + 1)
                    nc.vector.tensor_tensor(TA[:], MI[:, 0:M], SMU[:, b % 2, :], ALU.mult).then_inc(s_mi, 1)
                    dve.wait_ge(s_mi, mi_use[it] + 1)
                    link(nc.vector.tensor_tensor(TC[:], TA[:], NG[:, b, :], ALU.add))
                    link(nc.vector.tensor_reduce(MX[:], TC[:], AX_X, ALU.max))
                    if j:
                        dve.wait_ge(s_e, 2 * j)
                    nc.vector.tensor_scalar(TD[:], TC[:], MX[:], None, ALU.subtract).then_inc(s_t4, 1)
                elif kind == "T2":
                    dve.wait_ge(s_pa, j + 1)
                    nc.vector.tensor_tensor(PA[M:P, :], MI[M:P, 0:P], PA[M:P, :].bitcast(F32),
                                            ALU.subtract).then_inc(s_mi, 1)
                elif kind == "R":
                    link(nc.vector.reciprocal(RC[:], SM[:, j % 4:j % 4 + 1]))
                    for h in range(2):
                        dve.wait_ge(s_rw, 2 * j + h + 1)
                        xs = X[:, j % NX, 512 * h:512 * h + 512]
                        nc.vector.scalar_tensor_tensor(out=xs, in0=RP[:, h, :], scalar=RC[:], in1=xs,
                                                       op0=ALU.mult, op1=ALU.add).then_inc(s_rr, 1)
                    dve.wait_ge(s_rr, 2 * j + 2)
                    stats(B2, V2, j, X[:, j % NX, :], s_v2)
                elif kind == "U":
                    u = mn_use[it]
                    _, j, c0, w = it
                    dve.wait_ge(s_pe, u + 1)
                    dve.wait_ge(s_bi, j + 1)
                    for o in range(0, w, QW):
                        q = (c0 + o) // QW
                        xs = X[:, j % NX, c0 + o:c0 + o + QW]
                        last = nc.vector.scalar_tensor_tensor(out=xs, in0=MN[:, u % NM, o:o + QW],
                                                              scalar=AL[:, q:q + 1], in1=xs,
                                                              op0=ALU.mult, op1=ALU.add)
                    last.then_inc(s_mn, 1)
                elif kind == "WP":
                    m = mn_use[it]
                    q, c = divmod(j, C)
                    dve.wait_ge(s_ws, m + 1)
                    nc.vector.tensor_reduce(AM[:, q, c:c + 1], MN[:, m % NM, 0:QW], AX_X, ALU.max,
                                            apply_absolute_value=True).then_inc(s_mn, 1)
                elif kind == "WD":
                    q, c = divmod(j, C)
                    g = WG[:, j % NS]
                    dve.wait_ge(s_wg[j % NS], 16 * (j // NS + 1))
                    link(nc.vector.tensor_tensor(g[:, 0:4], g[:, 0:4], g[:, 4:8], ALU.add))
                    link(nc.vector.tensor_tensor(g[:, 0:2], g[:, 0:2], g[:, 2:4], ALU.add))
                    if q >= 2:
                        dve.wait_ge(s_wl, q - 1)
                        dve.wait_ge(s_wh, q - 1)
                    nc.vector.tensor_tensor(WF[:, q % 2, c, :], g[:, 0], g[:, 1], ALU.add).then_inc(s_wd, 1)
                    dve.wait_ge(s_wd, wd_done[j])
                    link(nc.vector.tensor_reduce(AM[:, q, c:c + 1], WF[:, q % 2, c, :], AX_X, ALU.max,
                                                 apply_absolute_value=True))
                elif kind == "CVT":
                    q = j
                    if q == 0:
                        dve.wait_ge(s_mn, C)
                    nc.vector.tensor_reduce(A1[:, q:q + 1], AM[:, q, :], AX_X, ALU.max).then_inc(s_am, 1)
                    dve.wait_ge(s_ar, q + 1)
                    a2, a3 = A2[:, q:q + 1], A3[:, q:q + 1]
                    link(nc.vector.tensor_scalar(a2, a2, TINY, None, ALU.max))
                    link(nc.vector.tensor_single_scalar(a3.bitcast(I32), a2.bitcast(I32), 0x7F800000,
                                                        ALU.bitwise_and))
                    link(nc.vector.reciprocal(SW[:, q:q + 1], a3))
                    nc.vector.tensor_scalar(SW[:, q:q + 1], SW[:, q:q + 1], WS_, None,
                                            ALU.mult).then_inc(s_sw, 1)
                    link(nc.vector.tensor_scalar(AL[:, q:q + 1], a3, float(NR) ** -0.5 / XS / WS_, None,
                                                 ALU.mult))
                    dve.wait_ge(s_wh, q + 1)
                    cols = slice(q * QW, (q + 1) * QW)
                    nc.vector.scalar_tensor_tensor(out=WL[:, :, cols], in0=WF[:, q % 2], scalar=SW[:, q:q + 1],
                                                   in1=WH[:, :, cols], op0=ALU.mult,
                                                   op1=ALU.subtract).then_inc(s_wl, 1)
                elif kind == "CTX":
                    b = j
                    dve.wait_ge(s_cx, 32 * (b + 1))
                    link(nc.vector.tensor_reduce(K1[:, 0:1], CX[0:M, :], AX_X, ALU.max,
                                                 apply_absolute_value=True))
                    link(nc.vector.tensor_scalar(K1[:, 1:2], K1[:, 0:1], TINY, None, ALU.max))
                    link(nc.vector.tensor_single_scalar(K1[:, 2:3].bitcast(I32), K1[:, 1:2].bitcast(I32),
                                                        0x7F800000, ALU.bitwise_and))
                    link(nc.vector.reciprocal(K1[:, 3:4], K1[:, 2:3]))
                    nc.vector.tensor_scalar(K1[:, 4:5], K1[:, 3:4], WS_, None, ALU.mult).then_inc(s_c1, 1)
                    link(nc.vector.tensor_scalar(K1[:, 5:6], K1[:, 2:3], float(D) ** -0.5 / XS / WS_, None,
                                                 ALU.mult))
                    if b:
                        dve.wait_ge(s_mw, mi_use[("CTX", b - 1)] + 1)
                    nc.vector.tensor_scalar(DG[:], ID[0:M, 0:M], K1[:, 5:6], None, ALU.mult).then_inc(s_dg, 1)
                    dve.wait_ge(s_ch, b + 1)
                    nc.vector.scalar_tensor_tensor(out=CL[:, b % 2, :], in0=CX[0:M, :], scalar=VA[0:M, b:b + 1],
                                                   in1=CH[0:M, b % 2, :].bitcast(F32), op0=ALU.mult,
                                                   op1=ALU.subtract).then_inc(s_cl, 1)
                    dve.wait_ge(s_mw, mi_use[it] + 1)
                    nc.vector.tensor_tensor(SMU[:, b % 2, :], MI[:, 0:M], MF[:, b, :], ALU.mult).then_inc(s_mi, 1)
                    dve.wait_ge(s_mi, mi_use[it] + 1)
                    n = tp_use[it]
                    low(n, CTL[:, b % 2], TP[:, n % 2, :], CTH[:, b % 2])

        @block.tensor
        def _(pe):
            pe.wait_ge(s_id, 1)
            pe.wait_ge(s_one, 1)

            def turn(n, src, h):
                if n >= 2:
                    pe.wait_ge(s_tl, n - 1)
                for c in range(4):
                    cc = 4 * h + c
                    mm = nc.tensor.transpose(TP[:, n % 2, c * P:(c + 1) * P], src[:, cc * P:(cc + 1) * P], ID[:])
                mm.then_inc(s_tw, 1)

            for it in items:
                kind = it[0]
                j = it[1]
                if kind == "T1":
                    pe.wait_ge(s_xn, j + 1)
                    for h in range(2):
                        turn(tp_use[it] + h, XN, h)
                elif kind == "T3":
                    pe.wait_ge(s_x1, j + 1)
                    for h in range(2):
                        turn(tp_use[it] + h, X1N, h)
                elif kind == "S":
                    b = j // TB
                    pe.wait_ge(s_tl, tp_use[("T1", j)] + 2)
                    pe.wait_ge(s_tl, tp_use[("CTX", b)] + 1)
                    pe.wait_ge(s_mi, mi_use[it])
                    for c in range(C):
                        for k, (a, w) in enumerate(((XH, CTH), (XH, CTL), (XL, CTH))):
                            mm = nc.tensor.matmul(MI[:, 0:M], a[:, c, :], w[:, b % 2, c, :],
                                                  start=(c == 0 and k == 0), stop=(c == C - 1 and k == 2))
                    mm.then_inc(s_mw, 1)
                elif kind == "T2":
                    pe.wait_ge(s_e, 2 * j + 2)
                    pe.wait_ge(s_mi, mi_use[it])
                    nc.tensor.transpose(MI[:, 0:P], PP[:], ID[:]).then_inc(s_mw, 1)
                elif kind == "R":
                    b = j // TB
                    pe.wait_ge(s_mi, mi_use[("T2", j)] + 1)
                    pe.wait_ge(s_cl, b + 1)
                    pe.wait_ge(s_ch, b + 1)
                    for h in range(2):
                        if j:
                            pe.wait_ge(s_rr, 2 * j - 1 + h)
                        cols = slice(512 * h, 512 * h + 512)
                        nc.tensor.matmul(RP[:, h, :], PA[:], CH[:, b % 2, cols], start=True, stop=False)
                        nc.tensor.matmul(RP[:, h, :], PA[0:M, :], CL[:, b % 2, cols],
                                         start=False, stop=True).then_inc(s_rw, 1)
                elif kind == "U":
                    u = mn_use[it]
                    _, j, c0, w = it
                    if u >= NM:
                        pe.wait_ge(s_mn, u - NM + 1)
                    pe.wait_ge(s_wl, (c0 + w) // QW)
                    pe.wait_ge(s_tl, tp_use[("T3", j)] + 2)
                    for c in range(C):
                        for k, (a, b) in enumerate(((YH, WH), (YH, WL), (YL, WH))):
                            mm = nc.tensor.matmul(MN[:, u % NM, 0:w], a[:, j % NXT, c, :], b[:, c, c0:c0 + w],
                                                  start=(c == 0 and k == 0), stop=(c == C - 1 and k == 2))
                    mm.then_inc(s_pe, 1)
                elif kind == "WP":
                    m = mn_use[it]
                    if m >= NM:
                        pe.wait_ge(s_mn, m - NM + 1)
                    pe.wait_ge(s_wg[j % NS], 16 * (j // NS + 1))
                    for r in range(NR):
                        mm = nc.tensor.matmul(MN[:, m % NM, 0:QW], ID[:], WG[:, j % NS, r, :],
                                              start=(r == 0), stop=(r == NR - 1))
                    mm.then_inc(s_pe, 1)
                elif kind == "CTX":
                    b = j
                    n = tp_use[it]
                    pe.wait_ge(s_cs, b + 1)
                    if n >= 2:
                        pe.wait_ge(s_tl, n - 1)
                    for c in range(C):
                        mm = nc.tensor.transpose(TP[:, n % 2, c * M:(c + 1) * M], CS[:, c * P:(c + 1) * P],
                                                 ID[0:M, 0:M])
                    mm.then_inc(s_tw, 1)
                    pe.wait_ge(s_dg, b + 1)
                    pe.wait_ge(s_mi, mi_use[it])
                    nc.tensor.matmul(MI[:, 0:M], ONE[0:M, :], DG[:], start=True, stop=True).then_inc(s_mw, 1)


_INS = ["x", "ctx_2048", "mask_BxS2_bk0", "L0_ffn_factors", "L0_ffn_bias"]


def kernel(**inputs):
    import numpy as _np
    import concourse.bacc as _bacc
    from concourse import mybir as _mybir
    from concourse.bass_utils import run_bass_kernel_spmd as _run

    nc = _bacc.Bacc("TRN2", target_bir_lowering=False, num_devices=1)
    arrays, args = {}, []
    for name in _INS:
        a = _np.ascontiguousarray(inputs[name])
        arrays[f"in_{name}_dram"] = a
        args.append(nc.dram_tensor(f"in_{name}_dram", a.shape, _mybir.dt.from_np(a.dtype), kind="ExternalInput").ap())
    args.append(nc.dram_tensor("out_0_dram", (8, 1024, 1024), _mybir.dt.float32, kind="ExternalOutput").ap())
    xattn_ffn_kernel(nc, *args)
    r = _run(nc, [arrays], core_ids=[0])
    return r.results[0]["out_0_dram"]
```

```python
from contextlib import ExitStack

import concourse.bass as bass
from concourse import mybir

ALU = mybir.AluOpType
ACT = mybir.ActivationFunctionType
F32 = mybir.dt.float32
F32R = mybir.dt.float32r
F16 = mybir.dt.float16
U8 = mybir.dt.uint8
I32 = mybir.dt.int32
AX_X = mybir.AxisListType.X
RMAX = bass.bass_isa.ReduceOp.max

P = 128
D = 1024
M = 64
NB = 8
NT = 64
TB = NT // NB
C = D // P
NR = 8
QW = 256
NQ = D // QW
NX = 9
NXT = 8
NPRO = 7
NS = 4
PE_SUMS = (0, 1, 2, 4, 5, 7)
POOL_SUMS = tuple(range(9, 32, 2))
NM = 3
NLD = 8
EPS = 1e-5
XS = 2.0 ** 10
WS_ = 2.0 ** 14
TINY = 2.0 ** -80


def schedule():
    items = []

    def put(*it):
        if it[1] < (NB if it[0] in ("CTXA", "CTXB") else NT) and it[1] >= 0 and it not in items:
            items.append(it)

    def step(k, units=(), ahead=True, lag=2, fill=lambda: None):
        put("ST", k)
        put("XN", k)
        items.extend(units[:1])
        fill()
        put("T1", k)
        put("T2", k - 1)
        if (k + 1) % TB == 0:
            put("CTXB", (k + 1) // TB)
        if ahead:
            put("ST", k + 1)
        put("X1N", k - 2)
        if ahead:
            put("XN", k + 1)
        if (k + 2) % TB == 0:
            put("CTXA", (k + 2) // TB)
        items.extend(units[1:])
        fill()
        for j in range(k - 3, k - lag + 1):
            put("T3", j)
        put("S", k)
        fill()
        for j in range(k - 3, k - lag + 1):
            put("BIAS", j)
        put("R", k - 1)
        fill()

    sums = [0]
    since = {}
    left = [(q, j) for q in range(NQ) for j in range(NPRO)]

    def load_weights():
        n = sums[0]
        if n <= NQ * C + 1:
            if n and n <= NQ * C:
                items.append(("AB", n - 1))
                if n % C == 0:
                    items.append(("CVT", n // C - 1))
            if n % C == 1 and n > 1:
                items.append(("CVL", n // C - 1))
            for m in range(n, n + 2):
                if m in POOL_SUMS and ("W1", m) not in items:
                    items.append(("W1", m))
            if n < NQ * C:
                items.append(("WP" if n in PE_SUMS else "WD", n))
            sums[0] += 1
        for it in items:
            since.setdefault(it, n)
        for q, j in left:
            if since.get(("CVL", q), n) + 1 <= n and since.get(("T3", j), n) + 1 <= n:
                items.append(("U", j, q * QW, QW))
                left.remove((q, j))
                break

    put("ST", 0)
    put("CTXA", 0)
    put("CTXB", 0)
    k = 0
    while k < NX:
        step(k, ahead=k + 1 < NX, lag=3, fill=load_weights)
        k += 1
    put("X1N", NX - 2)
    for j in range(NPRO):
        put("T3", j)
        put("BIAS", j)
        load_weights()
    while sums[0] <= NQ * C + 1:
        load_weights()
    for i in range(NPRO):
        for q, j in list(left):
            if j == i:
                items.append(("U", j, q * QW, QW))
        if i in (3, 5):
            step(k, ahead=i == 5)
            k += 1
    for i in range(NPRO, NT):
        step(k, (("U", i, 0, 512), ("U", i, 512, 512)))
        k += 1
    return items


def xattn_ffn_kernel(nc, x, ctx_in, mask, fac, bias, out):
    items = schedule()
    tp_use, mi_use, mn_use, units = {}, {}, {}, {}
    n_tp = n_mi = n_mn = 0
    for it in items:
        if it[0] in ("T1", "T3"):
            tp_use[it] = n_tp
            n_tp += 2
        elif it[0] == "CTXB":
            tp_use[it] = n_tp
            n_tp += 1
        if it[0] in ("S", "T2", "CTXB"):
            mi_use[it] = n_mi
            n_mi += 1
        if it[0] in ("WP", "U"):
            mn_use[it] = n_mn
            if it[0] == "U":
                units[it[1]] = n_mn
            n_mn += 1
    for it in items:
        assert items.count(it) == 1
    w1_done = {n: i + 1 for i, n in enumerate(POOL_SUMS)}
    wd_done = {}
    for it in items:
        if it[0] == "WD":
            wd_done[it[1]] = len(wd_done) + 1

    with ExitStack() as ctx:
        def sb(name, shape, dt):
            return ctx.enter_context(nc.sbuf_tensor(name, shape, dt))

        def ps(name, shape, dt):
            return ctx.enter_context(nc.psum_tensor(name, shape, dt))

        def sem(name):
            return ctx.enter_context(nc.semaphore(name))

        WH = sb("WH", [P, C, D], F16)
        WL = sb("WL", [P, C, D], F16)
        WG = sb("WG", [P, NS, NR, QW], F32)
        WF = sb("WF", [P, 2, C, QW], F32)
        X = sb("X", [P, NX, D], F32)
        XN = sb("XN", [P, D], F32)
        X1N = sb("X1N", [P, D], F32)
        XH = sb("XH", [P, C, P], F16)
        XL = sb("XL", [P, C, P], F16)
        YH = sb("YH", [P, NXT, C, P], F16)
        YL = sb("YL", [P, NXT, C, P], F16)
        CX = sb("CX", [P, D], F32)
        CS = sb("CS", [M, D], F32)
        CH = sb("CH", [P, 2, D], F32R)
        CL = sb("CL", [M, 2, D], F32R)
        CTH = sb("CTH", [P, 2, C, M], F16)
        CTL = sb("CTL", [P, 2, C, M], F16)
        BI = sb("BI", [P, D], F32)
        MU = sb("MU", [P, NB, M], U8)
        MF = sb("MF", [P, NB, M], F32)
        NG = sb("NG", [P, NB, M], F32)
        VA = sb("VA", [P, NB], F32)
        SMU = sb("SMU", [P, 2, M], F32)
        DG = sb("DG", [M, M], F32)
        ID = sb("ID", [P, P], F32)
        ONE = sb("ONE", [P, P], F32)
        PW = sb("PW", [P, 1], F32)
        TA = sb("TA", [P, M], F32)
        TC = sb("TC", [P, M], F32)
        TD = sb("TD", [P, M], F32)
        MX = sb("MX", [P, 1], F32)
        PP = sb("PP", [P, 2 * M], F32)
        PA = sb("PA", [P, P], F32R)
        SM = sb("SM", [P, 4], F32)
        RC = sb("RC", [P, 1], F32)
        B1 = sb("B1", [P, 2, 6], F32)
        B2 = sb("B2", [P, 2, 6], F32)
        V1 = sb("V1", [P, 4, 4], F32)
        V2 = sb("V2", [P, 4, 4], F32)
        G1 = sb("G1", [P, 4, 2], F32)
        G2 = sb("G2", [P, 4, 2], F32)
        AM = sb("AM", [P, NQ, C], F32)
        AB = sb("AB", [P, QW], F32)
        A1 = sb("A1", [P, NQ], F32)
        A2 = sb("A2", [P, NQ], F32)
        A3 = sb("A3", [P, NQ], F32)
        SW = sb("SW", [P, NQ], F32)
        AL = sb("AL", [P, NQ], F32)
        K1 = sb("K1", [M, 8], F32)

        MN = ps("MN", [P, NM, 512], F32)
        TP = ps("TP", [P, 2, 512], F32)
        RP = ps("RP", [P, 2, 512], F32)
        MI = ps("MI", [P, 512], F32)

        s_ld = [sem(f"s_ld{i}") for i in range(NX)]
        s_st = [sem(f"s_st{i}") for i in range(NX)]
        s_wg = [sem(f"s_wg{i}") for i in range(NS)]
        s_cx = sem("s_cx")
        s_bm = sem("s_bm")
        s_mk = sem("s_mk")
        s_id0 = sem("s_id0")
        s_id = sem("s_id")
        s_one = sem("s_one")
        s_v1 = sem("s_v1")
        s_v2 = sem("s_v2")
        s_p1 = sem("s_p1")
        s_p2 = sem("s_p2")
        s_xn = sem("s_xn")
        s_x1 = sem("s_x1")
        s_bi = sem("s_bi")
        s_tw = sem("s_tw")
        s_th = sem("s_th")
        s_tl = sem("s_tl")
        s_mw = sem("s_mw")
        s_mi = sem("s_mi")
        s_pe = sem("s_pe")
        s_mn = sem("s_mn")
        s_t4 = sem("s_t4")
        s_e = sem("s_e")
        s_pa = sem("s_pa")
        s_rw = sem("s_rw")
        s_rr = sem("s_rr")
        s_wd = sem("s_wd")
        s_w1 = sem("s_w1")
        s_ab = sem("s_ab")
        s_am = sem("s_am")
        s_ar = sem("s_ar")
        s_sw = sem("s_sw")
        s_wh = sem("s_wh")
        s_wl = sem("s_wl")
        s_c1 = sem("s_c1")
        s_cs = sem("s_cs")
        s_ch = sem("s_ch")
        s_cl = sem("s_cl")
        s_dg = sem("s_dg")
        s_vc = sem("s_vc")
        s_pc = sem("s_pc")

        xt = x.rearrange("b s d -> (b s) d").rearrange("(n p) d -> n p d", p=P)
        ot = out.rearrange("b s d -> (b s) d").rearrange("(n p) d -> n p d", p=P)
        ft = fac.rearrange("r (c p) (q e) -> q c p r e", p=P, e=QW)

        block = ctx.enter_context(nc.Block())

        @block.sync
        def _(sp):
            stored = [0]

            def load_x(j):
                if j >= NX:
                    sp.wait_ge(s_st[j % NX], 16 * (j // NX))
                sp.dma_start(X[:, j % NX, :], xt[j]).then_inc(s_ld[j % NX], 16)

            def load_ctx(b):
                if b:
                    sp.wait_ge(s_cl, b)
                    sp.wait_ge(s_ch, b)
                    sp.wait_ge(s_cs, b)
                sp.dma_start(CX[0:M, :], ctx_in[b]).then_inc(s_cx, 16)
                sp.dma_start(CX[M:P, :], ctx_in[b]).then_inc(s_cx, 16)

            def load_w(n):
                if n >= NS:
                    o = n - NS
                    if o in wd_done:
                        sp.wait_ge(s_wd, wd_done[o])
                    else:
                        sp.wait_ge(s_pe, mn_use[("WP", o)] + 1)
                sp.dma_start(WG[:, n % NS], ft[n // C, n % C]).then_inc(s_wg[n % NS], 16)

            def store(j):
                sp.wait_ge(s_mn, units[j] + 1)
                sp.dma_start(ot[j], X[:, j % NX, :]).then_inc(s_st[j % NX], 16)

            load_w(0)
            load_x(0)
            load_ctx(0)
            load_w(1)
            sp.dma_start(MU[:], mask.rearrange("b m -> (b m)").partition_broadcast(P)).then_inc(s_mk, 16)
            nx = 1
            for n in range(2, NQ * C):
                load_w(n)
                if (n in (2, 4, 5, 6) or n > 7) and nx < NX:
                    load_x(nx)
                    nx += 1
                if n == 4:
                    sp.dma_start(BI[:], bias.partition_broadcast(P)).then_inc(s_bm, 16)
                if n == 9:
                    load_ctx(1)
            for j in range(NT):
                store(j)
                if j + NX < NT:
                    load_x(j + NX)
                if (j + 9) % TB == 0 and 2 <= (j + 9) // TB < NB:
                    load_ctx((j + 9) // TB)
            for i in range(NX):
                sp.wait_ge(s_st[i], 16 * len(range(i, NT, NX)))

        @block.gpsimd
        def _(pool):
            nc.gpsimd.memset(ID[:], 0.0).then_inc(s_id0, 1)
            pool.wait_ge(s_id0, 1)
            nc.gpsimd.affine_select(out=ID[:], in_=ID[:], compare_op=ALU.not_equal, fill=1.0, base=0,
                                    pattern=[[-1, P]], channel_multiplier=1).then_inc(s_id, 1)
            nc.gpsimd.memset(ONE[:], 1.0).then_inc(s_one, 1)
            nc.gpsimd.memset(PW[:], -0.5).then_inc(s_pc, 1)
            chain = [1]
            pool.wait_ge(s_pc, 1)

            def scales(V, G, j, ready, done):
                pool.wait_ge(ready, j + 1)
                s = j % 4
                nc.gpsimd.tensor_tensor(G[:, s, 0:1], V[:, s, 3:4], PW[:], ALU.pow).then_inc(s_pc, 1)
                chain[0] += 1
                pool.wait_ge(s_pc, chain[0])
                nc.gpsimd.tensor_tensor(G[:, s, 1:2], V[:, s, 2:3], G[:, s, 0:1], ALU.mult).then_inc(done, 1)

            for it in items:
                if it[0] == "ST":
                    scales(V1, G1, it[1], s_v1, s_p1)
                elif it[0] == "R":
                    scales(V2, G2, it[1], s_v2, s_p2)
                elif it[0] == "BIAS":
                    j = it[1]
                    if j == 0:
                        pool.wait_ge(s_bm, 16)
                    pool.wait_ge(s_x1, j + 1)
                    xs = X[:, j % NX, :]
                    nc.gpsimd.tensor_tensor(xs, xs, BI[:], ALU.add).then_inc(s_bi, 1)
                elif it[0] == "W1":
                    n = it[1]
                    g = WG[:, n % NS]
                    pool.wait_ge(s_wg[n % NS], 16 * (n // NS + 1))
                    nc.gpsimd.tensor_tensor(g[:, 0:4], g[:, 0:4], g[:, 4:8], ALU.add).then_inc(s_w1, 1)
                elif it[0] == "CVT":
                    q = it[1]
                    pool.wait_ge(s_am, q + 1)
                    nc.gpsimd.partition_all_reduce(A2[:, q:q + 1], A1[:, q:q + 1], P, RMAX).then_inc(s_ar, 1)

        @block.scalar
        def _(act):
            def high(n, dst, src):
                act.wait_ge(s_tw, n + 1)
                nc.scalar.activation(dst, src, ACT.Copy).then_inc(s_th, 1)

            for it in items:
                kind = it[0]
                j = it[1]
                if kind == "XN":
                    act.wait_ge(s_p1, j + 1)
                    act.wait_ge(s_ld[j % NX], 16 * (j // NX + 1))
                    if j:
                        act.wait_ge(s_tw, tp_use[("T1", j - 1)] + 2)
                    nc.scalar.activation(XN[:], X[:, j % NX, :], ACT.Identity, bias=G1[:, j % 4, 1:2],
                                         scale=G1[:, j % 4, 0:1]).then_inc(s_xn, 1)
                elif kind == "X1N":
                    act.wait_ge(s_p2, j + 1)
                    if j:
                        act.wait_ge(s_tw, tp_use[("T3", j - 1)] + 2)
                    nc.scalar.activation(X1N[:], X[:, j % NX, :], ACT.Identity, bias=G2[:, j % 4, 1:2],
                                         scale=G2[:, j % 4, 0:1]).then_inc(s_x1, 1)
                elif kind == "T1":
                    n = tp_use[it]
                    if j:
                        act.wait_ge(s_mw, mi_use[("S", j - 1)] + 1)
                    for h in range(2):
                        high(n + h, XH[:, 4 * h:4 * h + 4, :], TP[:, (n + h) % 2, :])
                elif kind == "T3":
                    n = tp_use[it]
                    if j >= NXT:
                        act.wait_ge(s_pe, units[j - NXT] + 1)
                    for h in range(2):
                        high(n + h, YH[:, j % NXT, 4 * h:4 * h + 4, :], TP[:, (n + h) % 2, :])
                elif kind == "S":
                    act.wait_ge(s_t4, j + 1)
                    if j:
                        act.wait_ge(s_mw, mi_use[("T2", j - 1)] + 1)
                    nc.scalar.activation(PP[:, 0:M], TD[:], ACT.Exp,
                                         accum_out=SM[:, j % 4:j % 4 + 1]).then_inc(s_e, 1)
                    nc.scalar.activation(PP[:, M:2 * M], TD[:], ACT.Exp).then_inc(s_e, 1)
                elif kind == "T2":
                    act.wait_ge(s_mw, mi_use[it] + 1)
                    if j:
                        act.wait_ge(s_rw, 2 * j)
                    nc.scalar.activation(PA[:], MI[:, 0:P], ACT.Copy).then_inc(s_pa, 1)
                elif kind == "AB":
                    q, c = divmod(j, C)
                    if j in PE_SUMS:
                        act.wait_ge(s_mn, mn_use[("WP", j)] + 1)
                    else:
                        act.wait_ge(s_wd, wd_done[j])
                    if j:
                        act.wait_ge(s_ab, j)
                    nc.scalar.activation(AB[:], WF[:, q % 2, c, :], ACT.Abs,
                                         accum_out=AM[:, q, c:c + 1]).then_inc(s_ab, 1)
                elif kind == "CVT":
                    q = j
                    act.wait_ge(s_sw, q + 1)
                    nc.scalar.activation(WH[:, :, q * QW:(q + 1) * QW], WF[:, q % 2], ACT.Copy,
                                         scale=SW[:, q:q + 1]).then_inc(s_wh, 1)
                elif kind == "CTXA":
                    b = j
                    act.wait_ge(s_c1, b + 1)
                    if b:
                        act.wait_ge(s_tw, tp_use[("CTXB", b - 1)] + 1)
                    nc.scalar.activation(CS[:], CX[0:M, :], ACT.Copy, scale=K1[:, 4:5]).then_inc(s_cs, 1)
                    act.wait_ge(s_cx, 32 * (b + 1))
                    if b >= 2:
                        act.wait_ge(s_rw, 2 * TB * (b - 1))
                    nc.scalar.activation(CH[:, b % 2, :], CX[:], ACT.Copy, scale=VA[:, b:b + 1]).then_inc(s_ch, 1)
                elif kind == "CTXB":
                    n = tp_use[it]
                    high(n, CTH[:, j % 2], TP[:, n % 2, :])

        @block.vector
        def _(dve):
            chain = [0]

            def link(ins):
                chain[0] += 1
                ins.then_inc(s_vc, 1)
                dve.wait_ge(s_vc, chain[0])

            def low(n, dst, src, hi):
                dve.wait_ge(s_th, n + 1)
                nc.vector.tensor_tensor(dst, src, hi, ALU.subtract).then_inc(s_tl, 1)

            def stats(B, V, j, src, done):
                for h in range(2):
                    last = nc.vector.bn_stats(B[:, h, :], src[:, 512 * h:512 * h + 512])
                link(last)
                s = j % 4
                link(nc.vector.bn_aggr(V[:, s, 0:2], B[:]))
                nc.vector.tensor_scalar(V[:, s, 2:3], V[:, s, 0:1], -1.0, None, ALU.mult)
                nc.vector.tensor_scalar(V[:, s, 3:4], V[:, s, 1:2], EPS, XS ** -2, ALU.add,
                                        ALU.mult).then_inc(done, 1)

            dve.wait_ge(s_mk, 16)
            link(nc.vector.tensor_copy(MF[:], MU[:]))
            nc.vector.tensor_scalar(NG[:], MF[:], -1.0, 1e30, ALU.add, ALU.mult)
            link(nc.vector.tensor_reduce(VA[:], MF[:], AX_X, ALU.max))
            dve.wait_ge(s_id, 1)

            for it in items:
                kind = it[0]
                j = it[1]
                if kind == "ST":
                    dve.wait_ge(s_ld[j % NX], 16 * (j // NX + 1))
                    stats(B1, V1, j, X[:, j % NX, :], s_v1)
                elif kind == "T1":
                    n = tp_use[it]
                    for h in range(2):
                        c = slice(4 * h, 4 * h + 4)
                        low(n + h, XL[:, c, :], TP[:, (n + h) % 2, :], XH[:, c, :])
                elif kind == "T3":
                    n = tp_use[it]
                    for h in range(2):
                        c = slice(4 * h, 4 * h + 4)
                        low(n + h, YL[:, j % NXT, c, :], TP[:, (n + h) % 2, :], YH[:, j % NXT, c, :])
                elif kind == "S":
                    b = j // TB
                    dve.wait_ge(s_mw, mi_use[it] + 1)
                    nc.vector.tensor_tensor(TA[:], MI[:, 0:M], SMU[:, b % 2, :], ALU.mult).then_inc(s_mi, 1)
                    dve.wait_ge(s_mi, mi_use[it] + 1)
                    link(nc.vector.tensor_tensor(TC[:], TA[:], NG[:, b, :], ALU.add))
                    link(nc.vector.tensor_reduce(MX[:], TC[:], AX_X, ALU.max))
                    if j:
                        dve.wait_ge(s_e, 2 * j)
                    nc.vector.tensor_scalar(TD[:], TC[:], MX[:], None, ALU.subtract).then_inc(s_t4, 1)
                elif kind == "T2":
                    dve.wait_ge(s_pa, j + 1)
                    nc.vector.tensor_tensor(PA[M:P, :], MI[M:P, 0:P], PA[M:P, :].bitcast(F32),
                                            ALU.subtract).then_inc(s_mi, 1)
                elif kind == "R":
                    link(nc.vector.reciprocal(RC[:], SM[:, j % 4:j % 4 + 1]))
                    for h in range(2):
                        dve.wait_ge(s_rw, 2 * j + h + 1)
                        xs = X[:, j % NX, 512 * h:512 * h + 512]
                        nc.vector.scalar_tensor_tensor(out=xs, in0=RP[:, h, :], scalar=RC[:], in1=xs,
                                                       op0=ALU.mult, op1=ALU.add).then_inc(s_rr, 1)
                    dve.wait_ge(s_rr, 2 * j + 2)
                    stats(B2, V2, j, X[:, j % NX, :], s_v2)
                elif kind == "U":
                    u = mn_use[it]
                    _, j, c0, w = it
                    dve.wait_ge(s_pe, u + 1)
                    dve.wait_ge(s_bi, j + 1)
                    for o in range(0, w, QW):
                        q = (c0 + o) // QW
                        xs = X[:, j % NX, c0 + o:c0 + o + QW]
                        last = nc.vector.scalar_tensor_tensor(out=xs, in0=MN[:, u % NM, o:o + QW],
                                                              scalar=AL[:, q:q + 1], in1=xs,
                                                              op0=ALU.mult, op1=ALU.add)
                    last.then_inc(s_mn, 1)
                elif kind == "WP":
                    m = mn_use[it]
                    q, c = divmod(j, C)
                    dve.wait_ge(s_pe, m + 1)
                    nc.vector.tensor_copy(WF[:, q % 2, c, :], MN[:, m % NM, 0:QW]).then_inc(s_mn, 1)
                elif kind == "WD":
                    q, c = divmod(j, C)
                    g = WG[:, j % NS]
                    if j in w1_done:
                        dve.wait_ge(s_w1, w1_done[j])
                    else:
                        dve.wait_ge(s_wg[j % NS], 16 * (j // NS + 1))
                        link(nc.vector.tensor_tensor(g[:, 0:4], g[:, 0:4], g[:, 4:8], ALU.add))
                    link(nc.vector.tensor_tensor(g[:, 0:2], g[:, 0:2], g[:, 2:4], ALU.add))
                    if q >= 2:
                        dve.wait_ge(s_wl, q - 1)
                        dve.wait_ge(s_wh, q - 1)
                    nc.vector.tensor_tensor(WF[:, q % 2, c, :], g[:, 0], g[:, 1], ALU.add).then_inc(s_wd, 1)
                elif kind == "CVT":
                    q = j
                    dve.wait_ge(s_ab, C * (q + 1))
                    nc.vector.tensor_reduce(A1[:, q:q + 1], AM[:, q, :], AX_X, ALU.max).then_inc(s_am, 1)
                    dve.wait_ge(s_ar, q + 1)
                    a2, a3 = A2[:, q:q + 1], A3[:, q:q + 1]
                    link(nc.vector.tensor_scalar(a2, a2, TINY, None, ALU.max))
                    link(nc.vector.tensor_single_scalar(a3.bitcast(I32), a2.bitcast(I32), 0x7F800000,
                                                        ALU.bitwise_and))
                    link(nc.vector.reciprocal(SW[:, q:q + 1], a3))
                    nc.vector.tensor_scalar(SW[:, q:q + 1], SW[:, q:q + 1], WS_, None,
                                            ALU.mult).then_inc(s_sw, 1)
                    link(nc.vector.tensor_scalar(AL[:, q:q + 1], a3, float(NR) ** -0.5 / XS / WS_, None,
                                                 ALU.mult))
                elif kind == "CVL":
                    q = j
                    dve.wait_ge(s_wh, q + 1)
                    cols = slice(q * QW, (q + 1) * QW)
                    nc.vector.scalar_tensor_tensor(out=WL[:, :, cols], in0=WF[:, q % 2], scalar=SW[:, q:q + 1],
                                                   in1=WH[:, :, cols], op0=ALU.mult,
                                                   op1=ALU.subtract).then_inc(s_wl, 1)
                elif kind == "CTXA":
                    b = j
                    dve.wait_ge(s_cx, 32 * (b + 1))
                    link(nc.vector.tensor_reduce(K1[:, 0:1], CX[0:M, :], AX_X, ALU.max,
                                                 apply_absolute_value=True))
                    link(nc.vector.tensor_scalar(K1[:, 1:2], K1[:, 0:1], TINY, None, ALU.max))
                    link(nc.vector.tensor_single_scalar(K1[:, 2:3].bitcast(I32), K1[:, 1:2].bitcast(I32),
                                                        0x7F800000, ALU.bitwise_and))
                    link(nc.vector.reciprocal(K1[:, 3:4], K1[:, 2:3]))
                    nc.vector.tensor_scalar(K1[:, 4:5], K1[:, 3:4], WS_, None, ALU.mult).then_inc(s_c1, 1)
                    link(nc.vector.tensor_scalar(K1[:, 5:6], K1[:, 2:3], float(D) ** -0.5 / XS / WS_, None,
                                                 ALU.mult))
                    if b:
                        dve.wait_ge(s_mw, mi_use[("CTXB", b - 1)] + 1)
                    nc.vector.tensor_scalar(DG[:], ID[0:M, 0:M], K1[:, 5:6], None, ALU.mult).then_inc(s_dg, 1)
                    dve.wait_ge(s_ch, b + 1)
                    nc.vector.scalar_tensor_tensor(out=CL[:, b % 2, :], in0=CX[0:M, :], scalar=VA[0:M, b:b + 1],
                                                   in1=CH[0:M, b % 2, :].bitcast(F32), op0=ALU.mult,
                                                   op1=ALU.subtract).then_inc(s_cl, 1)
                elif kind == "CTXB":
                    b = j
                    dve.wait_ge(s_mw, mi_use[it] + 1)
                    nc.vector.tensor_tensor(SMU[:, b % 2, :], MI[:, 0:M], MF[:, b, :], ALU.mult).then_inc(s_mi, 1)
                    dve.wait_ge(s_mi, mi_use[it] + 1)
                    n = tp_use[it]
                    low(n, CTL[:, b % 2], TP[:, n % 2, :], CTH[:, b % 2])

        @block.tensor
        def _(pe):
            pe.wait_ge(s_id, 1)
            pe.wait_ge(s_one, 1)

            def turn(n, src, h):
                if n >= 2:
                    pe.wait_ge(s_tl, n - 1)
                for c in range(4):
                    cc = 4 * h + c
                    mm = nc.tensor.transpose(TP[:, n % 2, c * P:(c + 1) * P], src[:, cc * P:(cc + 1) * P], ID[:])
                mm.then_inc(s_tw, 1)

            for it in items:
                kind = it[0]
                j = it[1]
                if kind == "T1":
                    pe.wait_ge(s_xn, j + 1)
                    for h in range(2):
                        turn(tp_use[it] + h, XN, h)
                elif kind == "T3":
                    pe.wait_ge(s_x1, j + 1)
                    for h in range(2):
                        turn(tp_use[it] + h, X1N, h)
                elif kind == "S":
                    b = j // TB
                    pe.wait_ge(s_tl, tp_use[("T1", j)] + 2)
                    pe.wait_ge(s_tl, tp_use[("CTXB", b)] + 1)
                    pe.wait_ge(s_mi, mi_use[it])
                    for c in range(C):
                        for k, (a, w) in enumerate(((XH, CTH), (XH, CTL), (XL, CTH))):
                            mm = nc.tensor.matmul(MI[:, 0:M], a[:, c, :], w[:, b % 2, c, :],
                                                  start=(c == 0 and k == 0), stop=(c == C - 1 and k == 2))
                    mm.then_inc(s_mw, 1)
                elif kind == "T2":
                    pe.wait_ge(s_e, 2 * j + 2)
                    pe.wait_ge(s_mi, mi_use[it])
                    nc.tensor.transpose(MI[:, 0:P], PP[:], ID[:]).then_inc(s_mw, 1)
                elif kind == "R":
                    b = j // TB
                    pe.wait_ge(s_mi, mi_use[("T2", j)] + 1)
                    pe.wait_ge(s_cl, b + 1)
                    pe.wait_ge(s_ch, b + 1)
                    for h in range(2):
                        if j:
                            pe.wait_ge(s_rr, 2 * j - 1 + h)
                        cols = slice(512 * h, 512 * h + 512)
                        nc.tensor.matmul(RP[:, h, :], PA[:], CH[:, b % 2, cols], start=True, stop=False)
                        nc.tensor.matmul(RP[:, h, :], PA[0:M, :], CL[:, b % 2, cols],
                                         start=False, stop=True).then_inc(s_rw, 1)
                elif kind == "U":
                    u = mn_use[it]
                    _, j, c0, w = it
                    if u >= NM:
                        pe.wait_ge(s_mn, u - NM + 1)
                    pe.wait_ge(s_wl, (c0 + w) // QW)
                    pe.wait_ge(s_tl, tp_use[("T3", j)] + 2)
                    for c in range(C):
                        for k, (a, b) in enumerate(((YH, WH), (YH, WL), (YL, WH))):
                            mm = nc.tensor.matmul(MN[:, u % NM, 0:w], a[:, j % NXT, c, :], b[:, c, c0:c0 + w],
                                                  start=(c == 0 and k == 0), stop=(c == C - 1 and k == 2))
                    mm.then_inc(s_pe, 1)
                elif kind == "WP":
                    m = mn_use[it]
                    if m >= NM:
                        pe.wait_ge(s_mn, m - NM + 1)
                    pe.wait_ge(s_wg[j % NS], 16 * (j // NS + 1))
                    for r in range(NR):
                        mm = nc.tensor.matmul(MN[:, m % NM, 0:QW], ID[:], WG[:, j % NS, r, :],
                                              start=(r == 0), stop=(r == NR - 1))
                    mm.then_inc(s_pe, 1)
                elif kind == "CTXB":
                    b = j
                    n = tp_use[it]
                    pe.wait_ge(s_cs, b + 1)
                    if n >= 2:
                        pe.wait_ge(s_tl, n - 1)
                    for c in range(C):
                        mm = nc.tensor.transpose(TP[:, n % 2, c * M:(c + 1) * M], CS[:, c * P:(c + 1) * P],
                                                 ID[0:M, 0:M])
                    mm.then_inc(s_tw, 1)
                    pe.wait_ge(s_dg, b + 1)
                    pe.wait_ge(s_mi, mi_use[it])
                    nc.tensor.matmul(MI[:, 0:M], ONE[0:M, :], DG[:], start=True, stop=True).then_inc(s_mw, 1)


_INS = ["x", "ctx_2048", "mask_BxS2_bk0", "L0_ffn_factors", "L0_ffn_bias"]


def kernel(**inputs):
    import numpy as _np
    import concourse.bacc as _bacc
    from concourse import mybir as _mybir
    from concourse.bass_utils import run_bass_kernel_spmd as _run

    nc = _bacc.Bacc("TRN2", target_bir_lowering=False, num_devices=1)
    arrays, args = {}, []
    for name in _INS:
        a = _np.ascontiguousarray(inputs[name])
        arrays[f"in_{name}_dram"] = a
        args.append(nc.dram_tensor(f"in_{name}_dram", a.shape, _mybir.dt.from_np(a.dtype), kind="ExternalInput").ap())
    args.append(nc.dram_tensor("out_0_dram", (8, 1024, 1024), _mybir.dt.float32, kind="ExternalOutput").ap())
    xattn_ffn_kernel(nc, *args)
    r = _run(nc, [arrays], core_ids=[0])
    return r.results[0]["out_0_dram"]
```
